# Optimizing a Trainium2 kernel written in Bass

```python
import numpy as np
import jax
import jax.numpy as jnp

def _softmax(x, axis=-1):
    return jax.nn.softmax(x, axis=axis)

def _gelu(x):
    return jax.nn.gelu(x, approximate=True)

def _silu(x):
    return jax.nn.silu(x)

def _sigmoid(x):
    return jax.nn.sigmoid(x)

def _layernorm(x, axis=-1, eps=1e-05):
    m = jnp.mean(x, axis=axis, keepdims=True)
    v = jnp.var(x, axis=axis, keepdims=True)
    return (x - m) / jnp.sqrt(v + eps)

def _scatter_add(tgt, idx, src, axis=0):
    return tgt.at[idx].add(src)

def _segment_sum(src, seg, n):
    return jax.ops.segment_sum(src, seg, n)
kernel_name = 'mk_rec_standalone_d1_rec_r8_263416'

def setup_inputs(seed: int=0):
    np.random.seed(seed)
    _w = jnp.asarray

    def _rec_inputs():
        import jax
        import jax.numpy as jnp
        _rk = jax.random.key(seed)
        r_dense_x = -0.00338568 + 1.0005 * jax.random.normal(jax.random.fold_in(_rk, 1), (2048, 13), jnp.float32)
        r_sparse_x = jnp.stack([jax.random.randint(jax.random.fold_in(jax.random.fold_in(_rk, 2), 0), (2048,), 2, 12500, jnp.int32), jax.random.randint(jax.random.fold_in(jax.random.fold_in(_rk, 2), 1), (2048,), 1, 99999, jnp.int32), jax.random.randint(jax.random.fold_in(jax.random.fold_in(_rk, 2), 2), (2048,), 0, 12500, jnp.int32), jax.random.randint(jax.random.fold_in(jax.random.fold_in(_rk, 2), 3), (2048,), 5, 12500, jnp.int32), jax.random.randint(jax.random.fold_in(jax.random.fold_in(_rk, 2), 4), (2048,), 20, 99993, jnp.int32), jax.random.randint(jax.random.fold_in(jax.random.fold_in(_rk, 2), 5), (2048,), 0, 99993, jnp.int32), jax.random.randint(jax.random.fold_in(jax.random.fold_in(_rk, 2), 6), (2048,), 2, 99999, jnp.int32), jax.random.randint(jax.random.fold_in(jax.random.fold_in(_rk, 2), 7), (2048,), 2, 99995, jnp.int32), jax.random.randint(jax.random.fold_in(jax.random.fold_in(_rk, 2), 8), (2048,), 0, 99999, jnp.int32), jax.random.randint(jax.random.fold_in(jax.random.fold_in(_rk, 2), 9), (2048,), 2, 99986, jnp.int32), jax.random.randint(jax.random.fold_in(jax.random.fold_in(_rk, 2), 10), (2048,), 4, 99999, jnp.int32), jax.random.randint(jax.random.fold_in(jax.random.fold_in(_rk, 2), 11), (2048,), 15, 99999, jnp.int32), jax.random.randint(jax.random.fold_in(jax.random.fold_in(_rk, 2), 12), (2048,), 0, 99989, jnp.int32), jax.random.randint(jax.random.fold_in(jax.random.fold_in(_rk, 2), 13), (2048,), 5, 99990, jnp.int32), jax.random.randint(jax.random.fold_in(jax.random.fold_in(_rk, 2), 14), (2048,), 2, 99996, jnp.int32), jax.random.randint(jax.random.fold_in(jax.random.fold_in(_rk, 2), 15), (2048,), 3, 99994, jnp.int32), jax.random.randint(jax.random.fold_in(jax.random.fold_in(_rk, 2), 16), (2048,), 0, 99998, jnp.int32), jax.random.randint(jax.random.fold_in(jax.random.fold_in(_rk, 2), 17), (2048,), 13, 99998, jnp.int32), jax.random.randint(jax.random.fold_in(jax.random.fold_in(_rk, 2), 18), (2048,), 10, 12498, jnp.int32), jax.random.randint(jax.random.fold_in(jax.random.fold_in(_rk, 2), 19), (2048,), 0, 99999, jnp.int32), jax.random.randint(jax.random.fold_in(jax.random.fold_in(_rk, 2), 20), (2048,), 0, 99995, jnp.int32), jax.random.randint(jax.random.fold_in(jax.random.fold_in(_rk, 2), 21), (2048,), 1, 99998, jnp.int32), jax.random.randint(jax.random.fold_in(jax.random.fold_in(_rk, 2), 22), (2048,), 1, 99997, jnp.int32), jax.random.randint(jax.random.fold_in(jax.random.fold_in(_rk, 2), 23), (2048,), 2, 99989, jnp.int32), jax.random.randint(jax.random.fold_in(jax.random.fold_in(_rk, 2), 24), (2048,), 6, 12500, jnp.int32), jax.random.randint(jax.random.fold_in(jax.random.fold_in(_rk, 2), 25), (2048,), 2, 99995, jnp.int32)], axis=1)
        return (r_dense_x, r_sparse_x)
    r_dense_x, r_sparse_x = _rec_inputs()

    def _L0_rec_setup():
        import jax, jax.numpy as jnp
        import numpy as np
        B, F, D, DENSE, CARD = (2048, 26, 64, 13, 12500)
        H_BOT, H_TOP = (8, 16)
        key = jax.random.key(seed)
        ks = jax.random.split(key, 12)
        dense_x = jax.random.normal(ks[0], (B, DENSE), dtype=jnp.float32)
        sparse_x = jax.random.randint(ks[1], (B, F), 0, CARD, dtype=jnp.int64)
        tables = jax.random.normal(ks[2], (F, CARD, D), dtype=jnp.float32) * 0.01
        w1 = jax.random.normal(ks[3], (DENSE, H_BOT), dtype=jnp.float32) * (1.0 / np.sqrt(DENSE))
        b1 = jnp.zeros((H_BOT,), dtype=jnp.float32)
        w2 = jax.random.normal(ks[4], (H_BOT, D), dtype=jnp.float32) * (1.0 / np.sqrt(H_BOT))
        b2 = jnp.zeros((D,), dtype=jnp.float32)
        top_in = F * D + D
        tw1 = jax.random.normal(ks[5], (top_in, H_TOP), dtype=jnp.float32) * (1.0 / np.sqrt(top_in))
        tb1 = jnp.zeros((H_TOP,), dtype=jnp.float32)
        tw2 = jax.random.normal(ks[6], (H_TOP, 1), dtype=jnp.float32) * (1.0 / np.sqrt(H_TOP))
        tb2 = jnp.zeros((1,), dtype=jnp.float32)
        return {'dense_x': dense_x, 'sparse_x': sparse_x, 'tables': tables, 'w1': w1, 'b1': b1, 'w2': w2, 'b2': b2, 'tw1': tw1, 'tb1': tb1, 'tw2': tw2, 'tb2': tb2}
    _L0_rec_all = _L0_rec_setup()
    _L0_rec_in = {k: v for k, v in _L0_rec_all.items() if k in ('tables', 'w1', 'b1', 'w2', 'b2', 'tw1', 'tb1', 'tw2', 'tb2')}
    del _L0_rec_all
    return {'r_dense_x': r_dense_x, 'r_sparse_x': r_sparse_x, 'L0_rec_tables': _L0_rec_in['tables'], 'L0_rec_w1': _L0_rec_in['w1'], 'L0_rec_b1': _L0_rec_in['b1'], 'L0_rec_w2': _L0_rec_in['w2'], 'L0_rec_b2': _L0_rec_in['b2'], 'L0_rec_tw1': _L0_rec_in['tw1'], 'L0_rec_tb1': _L0_rec_in['tb1'], 'L0_rec_tw2': _L0_rec_in['tw2'], 'L0_rec_tb2': _L0_rec_in['tb2']}

def reference(r_dense_x, r_sparse_x, L0_rec_tables, L0_rec_w1, L0_rec_b1, L0_rec_w2, L0_rec_b2, L0_rec_tw1, L0_rec_tb1, L0_rec_tw2, L0_rec_tb2):
    import jax
    import jax.numpy as jnp

    def _L0_rec_ref(dense_x, sparse_x, tables, w1, b1, w2, b2, tw1, tb1, tw2, tb2):
        import jax, jax.numpy as jnp
        import numpy as np
        B, F, D, DENSE, CARD = (2048, 26, 64, 13, 12500)
        H_BOT, H_TOP = (8, 16)
        dense_out = jnp.maximum(dense_x @ w1 + b1, 0.0) @ w2 + b2
        emb = jax.vmap(lambda t, idx: t[idx], in_axes=(0, 1), out_axes=1)(tables, sparse_x)
        interaction = jnp.concatenate([emb.reshape(emb.shape[0], -1), dense_out], axis=1)
        logits = jnp.maximum(interaction @ tw1 + tb1, 0.0) @ tw2 + tb2
        return jax.nn.sigmoid(logits)
    y = _L0_rec_ref(r_dense_x, r_sparse_x, L0_rec_tables, L0_rec_w1, L0_rec_b1, L0_rec_w2, L0_rec_b2, L0_rec_tw1, L0_rec_tb1, L0_rec_tw2, L0_rec_tb2)
    return y

_drawn_inputs = setup_inputs


def setup_inputs(seed=0):
    import zlib

    import numpy as np

    out = dict(_drawn_inputs(seed))
    spreads = {'L0_rec_b1': (0.0, 0.8), 'L0_rec_b2': (0.0, 2.0), 'L0_rec_tb1': (0.0, 0.271)}
    factors = {'r_dense_x': 3.165, 'L0_rec_tables': 28.457, 'L0_rec_w1': 2.884, 'L0_rec_w2': 3.049}
    for name, (base, spread) in spreads.items():
        noise = np.random.default_rng([zlib.crc32(name.encode()), seed]).standard_normal(out[name].shape)
        drawn = base * np.exp(spread * noise) if base else spread * noise
        out[name] = jnp.asarray(drawn.astype(out[name].dtype))
    for name, factor in factors.items():
        out[name] = (out[name] * factor).astype(out[name].dtype)
    return out
```

```python
import concourse.bass as bass
from concourse import mybir
from contextlib import ExitStack


def embedding_mlp_kernel(nc, dense_x, sparse_x, tables, w1, b1, w2, b2, tw1, tb1, tw2, tb2, out):
    f32, i32, u32 = mybir.dt.float32, mybir.dt.int32, mybir.dt.uint32
    ALU = mybir.AluOpType
    ACT = mybir.ActivationFunctionType

    P = 128
    B, DENSE = dense_x.shape
    F, CARD, D = tables.shape
    H_BOT, H_TOP = w1.shape[1], tw1.shape[1]
    TILES = B // P
    PER = P // D
    CHUNKS = F // PER
    SLOTS = 2
    PAIRS = TILES // SLOTS
    DMA = 16

    sparse_v = sparse_x.rearrange("(p t) f -> p (t f)", t=TILES)
    dense_v = dense_x.rearrange("(p t) k -> p (t k)", t=TILES)
    rows_v = tables.rearrange("f c d -> (f c) d")
    out_v = out.rearrange("(p t) o -> p (t o)", t=TILES)

    ctx = ExitStack()
    with ctx:
        def sb(name, shape, dt=f32):
            return ctx.enter_context(nc.sbuf_tensor(name, shape, dt))

        def pb(name, shape):
            return ctx.enter_context(nc.psum_tensor(name, shape, f32))

        def sem(name):
            return ctx.enter_context(nc.semaphore(name))

        sparse_sb = sb("sparse_sb", [P, TILES * F], i32)
        dense_sb = sb("dense_sb", [P, TILES * DENSE])
        w1_sb = sb("w1_sb", [P, H_BOT])
        b1_sb = sb("b1_sb", [H_BOT, 1])
        w2_sb = sb("w2_sb", [P, D])
        b2_sb = sb("b2_sb", [D, 1])
        tw1_emb = sb("tw1_emb", [P, CHUNKS, H_TOP])
        tw1_dense = sb("tw1_dense", [P, H_TOP])
        tb1_sb = sb("tb1_sb", [H_TOP, 1])
        tw2_sb = sb("tw2_sb", [P, 1])
        tb2_sb = sb("tb2_sb", [P, 1])
        identity = sb("identity", [P, P])
        field_base = sb("field_base", [P, F])
        wrap = sb("wrap", [P, F])
        wrapped = sb("wrapped", [P, F])
        row_index = sb("row_index", [P, SLOTS, F], i32)
        x_tile = sb("x_tile", [P, DENSE])
        xT = sb("xT", [P, P])
        bottomT = sb("bottomT", [P, P])
        dense_outT = sb("dense_outT", [P, P])
        emb = sb("emb", [P, SLOTS, F * D])
        embT = sb("embT", [P, SLOTS, P])
        topT = sb("topT", [P, P])
        result = sb("result", [P, TILES])

        embT_ps = [pb(f"embT_ps{k}", [P, 512]) for k in range(SLOTS)]
        bottom_ps = pb("bottom_ps", [P, 512])
        hidden_ps = [pb(f"hidden_ps{k}", [H_TOP, 512]) for k in range(SLOTS)]
        logits_ps = pb("logits_ps", [P, 512])

        sparse_loaded = sem("sparse_loaded")
        dense_loaded = sem("dense_loaded")
        weights_loaded = sem("weights_loaded")
        base_ready = sem("base_ready")
        weights_zeroed = sem("weights_zeroed")
        layers_zeroed = sem("layers_zeroed")
        identity_zeroed = sem("identity_zeroed")
        identity_ready = sem("identity_ready")
        index_step = sem("index_step")
        index_ready = sem("index_ready")
        gathered = [[sem(f"gathered_{k}_{c}") for c in range(CHUNKS)] for k in range(SLOTS)]
        x_ready = sem("x_ready")
        xT_in_psum = sem("xT_in_psum")
        xT_ready = sem("xT_ready")
        bottom_in_psum = sem("bottom_in_psum")
        bottom_ready = sem("bottom_ready")
        dense_out_in_psum = sem("dense_out_in_psum")
        dense_out_ready = sem("dense_out_ready")
        transposed = sem("transposed")
        embT_ready = sem("embT_ready")
        hidden_ready = sem("hidden_ready")
        top_ready = sem("top_ready")
        logits_ready = sem("logits_ready")
        result_ready = sem("result_ready")
        stored = sem("stored")

        WEIGHT_LOADS = 9
        INDEX_STEPS = 2

        block = ctx.enter_context(nc.Block())

        @block.sync
        def _(sp):
            sp.dma_start(sparse_sb[:, :], sparse_v).then_inc(sparse_loaded, DMA)
            sp.dma_start(dense_sb[:, :], dense_v).then_inc(dense_loaded, DMA)
            sp.wait_ge(weights_zeroed, 4)
            sp.dma_start(w1_sb[0:DENSE, :], w1).then_inc(weights_loaded, DMA)
            sp.dma_start(b1_sb[:, :], b1.rearrange("(h o) -> h o", o=1)).then_inc(weights_loaded, DMA)
            sp.dma_start(w2_sb[0:H_BOT, :], w2).then_inc(weights_loaded, DMA)
            sp.dma_start(b2_sb[:, :], b2.rearrange("(h o) -> h o", o=1)).then_inc(weights_loaded, DMA)
            sp.dma_start(tw1_dense[0:D, :], tw1[F * D:F * D + D, :]).then_inc(weights_loaded, DMA)
            sp.dma_start(tw1_emb[:, :, :],
                         tw1[0:F * D, :].rearrange("(c p) h -> p c h", p=P)).then_inc(weights_loaded, DMA)
            sp.dma_start(tb1_sb[:, :], tb1.rearrange("(h o) -> h o", o=1)).then_inc(weights_loaded, DMA)
            sp.dma_start(tw2_sb[0:H_TOP, :], tw2).then_inc(weights_loaded, DMA)
            sp.dma_start(tb2_sb[:, :], tb2.rearrange("(p o) -> p o", p=1).to_broadcast([P, 1]))\
              .then_inc(weights_loaded, DMA)
            sp.wait_ge(result_ready, 1)
            sp.dma_start(out_v, result[:, :]).then_inc(stored, DMA)
            sp.wait_ge(stored, DMA)

        @block.gpsimd
        def _(pool):
            pool.iota(field_base[:, :], [[CARD, F]], base=0, channel_multiplier=0,
                      allow_small_or_imprecise_dtypes=True).then_inc(base_ready, 1)
            pool.memset(identity[:, :], 0.0).then_inc(identity_zeroed, 1)
            pool.wait_ge(identity_zeroed, 1)
            pool.affine_select(out=identity[:, :], in_=identity[:, :], compare_op=ALU.not_equal, fill=1.0,
                               base=0, pattern=[[-1, P]], channel_multiplier=1).then_inc(identity_ready, 1)

            with pool.Fori(0, PAIRS) as pair:
                for k in range(SLOTS):
                    pool.wait_ge(index_ready, pair * SLOTS + (k + 1))
                    pool.nop(nofuse=True)
                    for f in range(F):
                        pool.indirect_dma_start(
                            out=emb[:, k, f * D:(f + 1) * D], out_offset=None,
                            in_=rows_v,
                            in_offset=bass.IndirectOffsetOnAxis(
                                ap=row_index[:, k, f:f + 1].bitcast(u32), axis=0),
                        ).then_inc(gathered[k][f // PER], DMA)

        @block.scalar
        def _(act):
            with act.Fori(0, PAIRS) as pair:
                for k in range(SLOTS):
                    for c in range(CHUNKS):
                        n = k * CHUNKS + c
                        act.wait_ge(transposed, pair * (SLOTS * CHUNKS) + (n + 1))
                        act.activation(embT[:, n % SLOTS, :], embT_ps[n % SLOTS][:, 0:P], ACT.Copy)\
                           .then_inc(embT_ready, 1)
            act.wait_ge(weights_loaded, WEIGHT_LOADS * DMA)
            act.wait_ge(logits_ready, TILES)
            act.activation(result[:, :], logits_ps[:, 0:TILES], ACT.Sigmoid, bias=tb2_sb[:, 0:1])\
               .then_inc(result_ready, 1)

        @block.vector
        def _(dve):
            def make_indices(tile, k):
                raw = sparse_sb[:, bass.ds(tile * F, F)]
                dve.tensor_scalar(wrap[:, :], raw, 0.0, float(CARD), ALU.is_lt, ALU.mult).then_inc(index_step, 1)
                dve.wait_ge(index_step, tile * INDEX_STEPS + 1)
                dve.scalar_tensor_tensor(wrapped[:, :], raw, float(-CARD), wrap[:, :], ALU.max, ALU.add)\
                   .then_inc(index_step, 1)
                dve.wait_ge(index_step, tile * INDEX_STEPS + 2)
                dve.scalar_tensor_tensor(row_index[:, k, :], wrapped[:, :], float(CARD - 1), field_base[:, :],
                                         ALU.min, ALU.add).then_inc(index_ready, 1)

            def tile_steps(tile, k, more):
                dve.tensor_copy(x_tile[:, :], dense_sb[:, bass.ds(tile * DENSE, DENSE)]).then_inc(x_ready, 1)
                dve.wait_ge(xT_in_psum, tile + 1)
                dve.tensor_copy(xT[0:DENSE, :], bottom_ps[0:DENSE, 0:P]).then_inc(xT_ready, 1)
                dve.wait_ge(bottom_in_psum, tile + 1)
                dve.tensor_scalar(bottomT[0:H_BOT, :], bottom_ps[0:H_BOT, 0:P], b1_sb[:, 0:1], 0.0, ALU.add, ALU.max)\
                   .then_inc(bottom_ready, 1)
                dve.wait_ge(dense_out_in_psum, tile + 1)
                dve.tensor_scalar(dense_outT[0:D, :], bottom_ps[0:D, 0:P], b2_sb[:, 0:1], None, ALU.add)\
                   .then_inc(dense_out_ready, 1)
                dve.wait_ge(hidden_ready, tile + 1)
                dve.tensor_scalar(topT[0:H_TOP, :], hidden_ps[k][:, 0:P], tb1_sb[:, 0:1], 0.0, ALU.add, ALU.max)\
                   .then_inc(top_ready, 1)
                if more:
                    make_indices(tile + SLOTS, k)

            for t in (w1_sb, w2_sb, tw1_dense, tw2_sb):
                dve.memset(t[:, :], 0.0).then_inc(weights_zeroed, 1)
            for t in (xT, bottomT, dense_outT, topT):
                dve.memset(t[:, :], 0.0).then_inc(layers_zeroed, 1)
            dve.wait_ge(sparse_loaded, DMA)
            dve.wait_ge(base_ready, 1)
            for k in range(SLOTS):
                make_indices(k, k)
            dve.wait_ge(dense_loaded, DMA)
            dve.wait_ge(weights_loaded, WEIGHT_LOADS * DMA)
            dve.wait_ge(layers_zeroed, 4)
            with dve.Fori(0, PAIRS - 1) as pair:
                for k in range(SLOTS):
                    tile_steps(pair * SLOTS + k, k, True)
            for k in range(SLOTS):
                tile_steps((PAIRS - 1) * SLOTS + k, k, False)

        @block.tensor
        def _(pe):
            pe.wait_ge(identity_ready, 1)
            pe.wait_ge(weights_loaded, WEIGHT_LOADS * DMA)
            with pe.Fori(0, PAIRS) as pair:
                for k in range(SLOTS):
                    tile = pair * SLOTS + k
                    pe.wait_ge(x_ready, tile + 1)
                    pe.transpose(bottom_ps[0:DENSE, 0:P], x_tile[:, :], identity[:, :]).then_inc(xT_in_psum, 1)
                    pe.wait_ge(xT_ready, tile + 1)
                    pe.matmul(bottom_ps[0:H_BOT, 0:P], w1_sb[:, :], xT[:, :], start=True, stop=True)\
                      .then_inc(bottom_in_psum, 1)
                    pe.wait_ge(bottom_ready, tile + 1)
                    pe.matmul(bottom_ps[0:D, 0:P], w2_sb[:, :], bottomT[:, :], start=True, stop=True)\
                      .then_inc(dense_out_in_psum, 1)
                    pe.wait_ge(dense_out_ready, tile + 1)
                    pe.matmul(hidden_ps[k][:, 0:P], tw1_dense[:, :], dense_outT[:, :], start=True, stop=False)
                    for c in range(CHUNKS):
                        n = k * CHUNKS + c
                        pe.wait_ge(gathered[k][c], pair * (PER * DMA) + PER * DMA)
                        pe.transpose(embT_ps[n % SLOTS][:, 0:P], emb[:, k, c * P:(c + 1) * P], identity[:, :])\
                          .then_inc(transposed, 1)
                        pe.wait_ge(embT_ready, pair * (SLOTS * CHUNKS) + (n + 1))
                        product = pe.matmul(hidden_ps[k][:, 0:P], tw1_emb[:, c, :], embT[:, n % SLOTS, :],
                                            start=False, stop=c == CHUNKS - 1)
                    product.then_inc(hidden_ready, 1)
                    pe.wait_ge(top_ready, tile + 1)
                    pe.matmul(logits_ps[:, bass.ds(tile, 1)], topT[:, :], tw2_sb[:, :], start=True, stop=True)\
                      .then_inc(logits_ready, 1)


_INS = ["r_dense_x", "r_sparse_x"] + ["L0_rec_" + n for n in
        ("tables", "w1", "b1", "w2", "b2", "tw1", "tb1", "tw2", "tb2")]


def kernel(**inputs):
    import numpy as _np
    import concourse.bacc as _bacc
    from concourse import mybir as _mybir
    from concourse.bass_utils import run_bass_kernel_spmd as _run

    nc = _bacc.Bacc("TRN2", target_bir_lowering=False, num_devices=1)
    arrays, args = {}, []
    for name in _INS:
        a = _np.ascontiguousarray(inputs[name])
        arrays[f"in_{name}"] = a
        args.append(nc.dram_tensor(f"in_{name}", a.shape, _mybir.dt.from_np(a.dtype), kind="ExternalInput").ap())
    out_shape = (inputs["r_dense_x"].shape[0], inputs["L0_rec_tw2"].shape[1])
    out = nc.dram_tensor("out", out_shape, _mybir.dt.float32, kind="ExternalOutput").ap()
    embedding_mlp_kernel(nc, *args, out)
    r = _run(nc, [arrays], core_ids=[0])
    return r.results[0]["out"]
```

```python
import concourse.bass as bass
from concourse import mybir
from contextlib import ExitStack


def embedding_mlp_kernel(nc, dense_x, sparse_x, tables, w1, b1, w2, b2, tw1, tb1, tw2, tb2, out):
    f32, bf16, i32, u32 = mybir.dt.float32, mybir.dt.bfloat16, mybir.dt.int32, mybir.dt.uint32
    ALU = mybir.AluOpType
    ACT = mybir.ActivationFunctionType
    AX = mybir.AxisListType

    P = 128
    B, DENSE = dense_x.shape
    F, CARD, D = tables.shape
    H_BOT, H_TOP = w1.shape[1], tw1.shape[1]
    TILES = B // P
    BANK = 512
    BANKS = B // BANK
    PER_BANK = BANK // P
    DMA = 16

    LOOKED_UP = 5
    GATHERED = F - LOOKED_UP
    PER_CHUNK = P // D
    CHUNKS = -(-GATHERED // PER_CHUNK)
    RING = 2 * CHUNKS
    ALL_CHUNKS = TILES * CHUNKS

    RUN = 4
    BLOCK = RUN * P
    BLOCKS = CARD // BLOCK
    REST = (CARD - BLOCKS * BLOCK) // RUN
    H = P // H_TOP
    GROUP_BLOCKS = H // RUN
    GROUP_ROWS = GROUP_BLOCKS * BLOCK
    GROUPS = -(-CARD // GROUP_ROWS)
    PAIRS = RUN * D // P
    STEPS = LOOKED_UP * GROUPS
    SPLITS = 3
    LEAD = 2
    SLOTS = LEAD + 1
    DIGITS = 3
    LO, G1, HH = range(DIGITS)
    assert GROUP_ROWS == 1024 and BLOCK == 512 and REST * RUN + BLOCKS * BLOCK == CARD

    def chunk_fields(c):
        return range(c * PER_CHUNK, min((c + 1) * PER_CHUNK, GATHERED))

    ARRIVE, AHEAD, MOST = 2.4, 8, 3
    chunks_of_step, taken = [], 0
    for j in range(STEPS):
        until = min(ALL_CHUNKS, taken + MOST, int(AHEAD + ARRIVE * j))
        chunks_of_step.append(list(range(taken, until)))
        taken = until
    last_chunks = range(taken, ALL_CHUNKS)

    def extent(g):
        blocks = min(GROUP_BLOCKS, BLOCKS + 1 - g * GROUP_BLOCKS)
        return (REST if g * GROUP_BLOCKS + blocks > BLOCKS else P), blocks

    def place(j):
        s, i = divmod(j, GROUPS)
        return s, {GROUPS - 1: GROUPS - 2, GROUPS - 2: GROUPS - 1}.get(i, i), i

    sparse_v = sparse_x.rearrange("(p t) f -> p (t f)", t=TILES)
    dense_v = dense_x.rearrange("(p t) k -> p (t k)", t=TILES)
    rows_v = tables.rearrange("f c d -> (f c) d")
    out_v = out.rearrange("(p t) o -> p (t o)", t=TILES)
    digits_dram = nc.dram_tensor("digits_dram", [LOOKED_UP, DIGITS * B], bf16, kind="Internal").ap()

    ctx = ExitStack()
    with ctx:
        def sb(name, shape, dt=f32):
            return ctx.enter_context(nc.sbuf_tensor(name, shape, dt))

        def pb(name):
            return ctx.enter_context(nc.psum_tensor(name, [P, BANK], f32))

        def sem(name):
            return ctx.enter_context(nc.semaphore(name))

        sparse_sb = sb("sparse_sb", [P, TILES * F], i32)
        dense_sb = sb("dense_sb", [P, TILES * DENSE])
        w1_sb = sb("w1_sb", [DENSE, H_BOT])
        b1_sb = sb("b1_sb", [H_BOT, 1])
        w2_sb = sb("w2_sb", [H_BOT, D])
        b2_sb = sb("b2_sb", [D, 1])
        tw1_emb = sb("tw1_emb", [P, CHUNKS, H_TOP])
        tw1_dense = sb("tw1_dense", [D, H_TOP])
        tw1_pair = sb("tw1_pair", [P, LOOKED_UP, 2 * H_TOP])
        tb1_row = sb("tb1_row", [1, TILES, H_TOP])
        tw2_all = sb("tw2_all", [P, TILES, H_TOP])
        tb2_sb = sb("tb2_sb", [P, 1])
        identity = sb("identity", [P, P])
        ones_row = sb("ones_row", [1, P])
        field_base = sb("field_base", [P, TILES, F])
        partition = sb("partition", [P, 1], i32)
        partition_f = sb("partition_f", [P, 1])
        part_h = sb("part_h", [P, 1], i32)
        part_unit = sb("part_unit", [P, 1], i32)
        part_h_f = sb("part_h_f", [P, 1])
        part_unit_f = sb("part_unit_f", [P, 1])
        unit = sb("unit", [P, H_TOP])
        add_h = sb("add_h", [P, H_TOP])
        wrap = sb("wrap", [P, TILES * F])
        wrapped = sb("wrapped", [P, TILES * F])
        row_index = sb("row_index", [P, TILES * F], i32)
        local = sb("local", [P, TILES, LOOKED_UP], i32)
        digit_i = sb("digit_i", [P, 4, TILES, LOOKED_UP], i32)
        digit_f = sb("digit_f", [P, TILES, DIGITS, LOOKED_UP])
        digit_rows = sb("digit_rows", [DIGITS * LOOKED_UP, B], bf16)
        digit_bc = sb("digit_bc", [P, 2, DIGITS * B], bf16)
        xT = sb("xT", [DENSE, BANK])
        bottomT = sb("bottomT", [H_BOT, BANK])
        dense_outT = sb("dense_outT", [D, B])
        emb = sb("emb", [P, RING, P])
        embT = sb("embT", [P, 2, P])
        table = sb("table", [P, 2, BLOCKS + 1, RUN * D])
        tableT = sb("tableT", [P, BANK])
        residual = sb("residual", [P, SLOTS, P])
        parts = sb("parts", [P, SLOTS, SPLITS, P], bf16)
        key = sb("key", [P, 2, B], bf16)
        onehot = sb("onehot", [P, SLOTS, B], bf16)
        picked = sb("picked", [P, B])
        picked_sum = sb("picked_sum", [P, B])
        weighted = sb("weighted", [P, TILES, H_TOP])
        logits = sb("logits", [P, TILES])
        result = sb("result", [P, TILES])

        hidden_ps = pb("hidden_ps")
        looked_ps = [pb(f"looked_ps{q}") for q in range(BANKS)]
        tableT_ps = pb("tableT_ps")
        chunks_ps = pb("chunks_ps")
        groups_ps = pb("groups_ps")

        def embT_ps(n):
            return chunks_ps[:, (n % 2) * P:(n % 2 + 1) * P]

        def projected_ps(j):
            return groups_ps[:, (j % 2) * P:(j % 2 + 1) * P]

        sparse_loaded = sem("sparse_loaded")
        dense_loaded = sem("dense_loaded")
        bottom_weights = sem("bottom_weights")
        top_weights = sem("top_weights")
        head_weights = sem("head_weights")
        pair_zeroed = sem("pair_zeroed")
        ones_ready = sem("ones_ready")
        base_ready = sem("base_ready")
        identity_zeroed = sem("identity_zeroed")
        identity_ready = sem("identity_ready")
        constants = sem("constants")
        dve_step = sem("dve_step")
        index_ready = sem("index_ready")
        digits_ready = sem("digits_ready")
        digits_in_psum = sem("digits_in_psum")
        digit_rows_ready = sem("digit_rows_ready")
        digits_stored = sem("digits_stored")
        digits_loaded = [sem(f"digits_loaded{k}") for k in range(2)]
        table_loaded = [sem(f"table_loaded{k}") for k in range(2)]
        bottom_in_psum = sem("bottom_in_psum")
        bottom_ready = sem("bottom_ready")
        gathered = [sem(f"gathered{r}") for r in range(RING)]
        emb_transposed = sem("emb_transposed")
        embT_ready = sem("embT_ready")
        table_transposed = sem("table_transposed")
        tableT_ready = sem("tableT_ready")
        projected = sem("projected")
        high_ready = sem("high_ready")
        residual_ready = sem("residual_ready")
        middle_ready = sem("middle_ready")
        parts_ready = sem("parts_ready")
        key_ready = sem("key_ready")
        onehot_ready = sem("onehot_ready")
        step_done = sem("step_done")
        picked_ready = sem("picked_ready")
        picked_summed = sem("picked_summed")
        hidden_ready = sem("hidden_ready")
        logits_ready = sem("logits_ready")
        result_ready = sem("result_ready")
        stored = sem("stored")

        TABLE_LOADS = 2
        BOTTOM_STAGES = 3

        def fill(sem_value):
            return sem_value * DMA

        block = ctx.enter_context(nc.Block())

        @block.sync
        def _(sp):
            def load_table(s):
                rows = tables[GATHERED + s]
                sp.dma_start(table[:, s % 2, 0:BLOCKS, :],
                             rows[0:BLOCKS * BLOCK, :].rearrange("(q p r) d -> p q (r d)", p=P, r=RUN))\
                  .then_inc(table_loaded[s % 2], DMA)
                sp.dma_start(table[0:REST, s % 2, BLOCKS, :],
                             rows[BLOCKS * BLOCK:CARD, :].rearrange("(p r) d -> p (r d)", r=RUN))\
                  .then_inc(table_loaded[s % 2], DMA)

            def load_digits(s):
                sp.dma_start(digit_bc[:, s % 2, :], digits_dram[s:s + 1, :].to_broadcast([P, DIGITS * B]))\
                  .then_inc(digits_loaded[s % 2], DMA)

            sp.dma_start(sparse_sb[:, :], sparse_v).then_inc(sparse_loaded, DMA)
            sp.dma_start(dense_sb[:, :], dense_v).then_inc(dense_loaded, DMA)
            load_table(0)
            sp.wait_ge(digit_rows_ready, BANKS)
            sp.dma_start(digits_dram.rearrange("s (g b) -> g s b", g=DIGITS), digit_rows[:, :])\
              .then_inc(digits_stored, DMA)
            sp.wait_ge(digits_stored, DMA)
            load_digits(0)
            load_table(1)
            load_digits(1)
            for s in range(2, LOOKED_UP):
                sp.wait_ge(table_transposed, (s - 1) * GROUPS)
                load_table(s)
                sp.wait_ge(picked_ready, (s - 1) * BANKS)
                load_digits(s)
            sp.wait_ge(result_ready, 1)
            sp.dma_start(out_v, result[:, :]).then_inc(stored, DMA)
            sp.wait_ge(stored, DMA)

        @block.gpsimd
        def _(pool):
            pool.iota(field_base[:, :, :], [[0, TILES], [CARD, F]], base=0, channel_multiplier=0,
                      allow_small_or_imprecise_dtypes=True).then_inc(base_ready, 1)
            pool.memset(identity[:, :], 0.0).then_inc(identity_zeroed, 1)
            pool.wait_ge(identity_zeroed, 1)
            pool.affine_select(out=identity[:, :], in_=identity[:, :], compare_op=ALU.not_equal, fill=1.0,
                               base=0, pattern=[[-1, P]], channel_multiplier=1).then_inc(identity_ready, 1)
            pool.iota(partition[:, :], [[0, 1]], base=0, channel_multiplier=1).then_inc(constants, 1)
            pool.iota(unit[:, :], [[1, H_TOP]], base=0, channel_multiplier=0,
                      allow_small_or_imprecise_dtypes=True).then_inc(constants, 1)
            for n in range(ALL_CHUNKS):
                tile, c = divmod(n, CHUNKS)
                if n < 2 * CHUNKS and c == 0:
                    pool.wait_ge(index_ready, tile + 1)
                if n >= RING:
                    pool.wait_ge(emb_transposed, n - RING + 1)
                for e, f in enumerate(chunk_fields(c)):
                    pool.indirect_dma_start(
                        out=emb[:, n % RING, e * D:(e + 1) * D], out_offset=None, in_=rows_v,
                        in_offset=bass.IndirectOffsetOnAxis(
                            ap=row_index[:, tile * F + f:tile * F + f + 1].bitcast(u32), axis=0),
                    ).then_inc(gathered[n % RING], DMA)

        @block.scalar
        def _(act):
            act.dma_start(w1_sb[:, :], w1).then_inc(bottom_weights, DMA)
            act.dma_start(b1_sb[:, :], b1.rearrange("(h o) -> h o", o=1)).then_inc(bottom_weights, DMA)
            act.dma_start(w2_sb[:, :], w2).then_inc(bottom_weights, DMA)
            act.dma_start(b2_sb[:, :], b2.rearrange("(h o) -> h o", o=1)).then_inc(bottom_weights, DMA)
            act.dma_start(tw1_dense[:, :], tw1[F * D:F * D + D, :]).then_inc(top_weights, DMA)
            act.dma_start(tb1_row[:, :, :], tb1.rearrange("(o t h) -> o t h", o=1, t=1)
                          .to_broadcast([1, TILES, H_TOP])).then_inc(top_weights, DMA)
            whole = GATHERED * D // P
            act.dma_start(tw1_emb[:, 0:whole, :], tw1[0:whole * P, :].rearrange("(c p) h -> p c h", p=P))\
               .then_inc(top_weights, DMA)
            act.dma_start(tw1_emb[0:GATHERED * D - whole * P, whole, :], tw1[whole * P:GATHERED * D, :])\
               .then_inc(top_weights, DMA)
            act.wait_ge(pair_zeroed, 1)
            for e in range(2):
                act.dma_start(tw1_pair[e * D:(e + 1) * D, :, e * H_TOP:(e + 1) * H_TOP],
                              tw1[GATHERED * D:F * D, :].rearrange("(s d) h -> d s h", d=D))\
                   .then_inc(top_weights, DMA)
            act.dma_start(tw2_all[:, :, :], tw2.rearrange("(p t h) o -> p t (h o)", p=1, t=1)
                          .to_broadcast([P, TILES, H_TOP])).then_inc(head_weights, DMA)
            act.dma_start(tb2_sb[:, :], tb2.rearrange("(p o) -> p o", p=1).to_broadcast([P, 1]))\
               .then_inc(head_weights, DMA)

            for q in range(BANKS):
                act.wait_ge(digits_in_psum, q + 1)
                act.activation(digit_rows[:, q * BANK:(q + 1) * BANK], looked_ps[q][0:DIGITS * LOOKED_UP, :],
                               ACT.Copy).then_inc(digit_rows_ready, 1)

            def table_steps(j):
                act.wait_ge(table_transposed, j + 1)
                act.activation(tableT[:, :], tableT_ps[:, :], ACT.Copy).then_inc(tableT_ready, 1)

            def high(j):
                act.wait_ge(projected, j + 1)
                if j >= SLOTS:
                    act.wait_ge(step_done, j - SLOTS + 1)
                act.activation(parts[:, j % SLOTS, 0, :], projected_ps(j), ACT.Copy)\
                   .then_inc(high_ready, 1)

            def middle(j):
                act.wait_ge(residual_ready, j + 1)
                act.activation(parts[:, j % SLOTS, 1, :], residual[:, j % SLOTS, :], ACT.Copy).then_inc(middle_ready, 1)

            def chunk(n):
                rows = len(chunk_fields(n % CHUNKS)) * D
                act.wait_ge(emb_transposed, n + 1)
                act.activation(embT[0:rows, n % 2, :], embT_ps(n)[0:rows, :], ACT.Copy)\
                   .then_inc(embT_ready, 1)

            for j in range(LEAD):
                table_steps(j)
                high(j)
                middle(j)
            for j in range(STEPS):
                if j + LEAD < STEPS:
                    table_steps(j + LEAD)
                for n in chunks_of_step[j][0:1]:
                    chunk(n)
                if j + LEAD < STEPS:
                    high(j + LEAD)
                for n in chunks_of_step[j][1:2]:
                    chunk(n)
                if j + LEAD < STEPS:
                    middle(j + LEAD)
                for n in chunks_of_step[j][2:]:
                    chunk(n)
            for n in last_chunks:
                chunk(n)
            act.wait_ge(head_weights, fill(2))
            act.wait_ge(logits_ready, 1)
            act.activation(result[:, :], logits[:, :], ACT.Sigmoid, bias=tb2_sb[:, 0:1]).then_inc(result_ready, 1)

        @block.vector
        def _(dve):
            done = [0]

            def link(instruction):
                done[0] += 1
                instruction.then_inc(dve_step, 1)
                dve.wait_ge(dve_step, done[0])

            dve.memset(tw1_pair[:, :, :], 0.0).then_inc(pair_zeroed, 1)
            dve.memset(ones_row[:, :], 1.0).then_inc(ones_ready, 1)
            dve.wait_ge(sparse_loaded, DMA)
            dve.wait_ge(base_ready, 1)
            base = field_base[:, :, :].rearrange("p t f -> p (t f)")
            for a, b in ((0, F), (F, TILES * F)):
                link(dve.tensor_scalar(wrap[:, a:b], sparse_sb[:, a:b], 0.0, float(CARD), ALU.is_lt, ALU.mult))
                link(dve.scalar_tensor_tensor(wrapped[:, a:b], sparse_sb[:, a:b], float(-CARD), wrap[:, a:b],
                                              ALU.max, ALU.add))
                dve.scalar_tensor_tensor(row_index[:, a:b], wrapped[:, a:b], float(CARD - 1), base[:, a:b],
                                         ALU.min, ALU.add).then_inc(index_ready, 1)

            link(dve.tensor_scalar(local[:, :, :],
                                   wrapped[:, :].rearrange("p (t f) -> p t f", f=F)[:, :, GATHERED:F],
                                   float(CARD - 1), None, ALU.min))
            g_i, lo_i, h1_i, h0_i = (digit_i[:, k, :, :] for k in range(4))
            link(dve.tensor_scalar(g_i, local[:, :, :], 10, None, ALU.logical_shift_right))
            link(dve.tensor_scalar(lo_i, local[:, :, :], 2, P - 1, ALU.logical_shift_right, ALU.bitwise_and))
            link(dve.tensor_scalar(h1_i, local[:, :, :], 7, RUN, ALU.logical_shift_right, ALU.bitwise_and))
            link(dve.tensor_scalar(h0_i, local[:, :, :], RUN - 1, None, ALU.bitwise_and))
            dve.tensor_scalar(digit_f[:, :, G1, :], g_i, 1.0, None, ALU.add).then_inc(digits_ready, 1)
            dve.tensor_copy(digit_f[:, :, LO, :], lo_i).then_inc(digits_ready, 1)
            dve.tensor_tensor(digit_f[:, :, HH, :], h1_i, h0_i, ALU.add).then_inc(digits_ready, 1)

            dve.wait_ge(constants, 2)
            link(dve.tensor_copy(partition_f[:, :], partition[:, :]))
            link(dve.tensor_scalar(part_h[:, :], partition[:, :], 4, None, ALU.logical_shift_right))
            link(dve.tensor_scalar(part_unit[:, :], partition[:, :], H_TOP - 1, None, ALU.bitwise_and))
            link(dve.tensor_copy(part_h_f[:, :], part_h[:, :]))
            link(dve.tensor_copy(part_unit_f[:, :], part_unit[:, :]))
            link(dve.tensor_scalar(add_h[:, :], unit[:, :], part_unit_f[:, 0:1], None, ALU.is_equal))

            dve.wait_ge(bottom_weights, fill(4))

            def bottom_stage(m):
                q, stage = divmod(m, BOTTOM_STAGES)
                dve.wait_ge(bottom_in_psum, m + 1)
                if stage == 0:
                    taken = dve.tensor_copy(xT[:, :], tableT_ps[0:DENSE, :])
                elif stage == 1:
                    taken = dve.tensor_scalar(bottomT[:, :], tableT_ps[0:H_BOT, :], b1_sb[:, 0:1], 0.0,
                                              ALU.add, ALU.max)
                else:
                    taken = dve.tensor_scalar(dense_outT[:, q * BANK:(q + 1) * BANK], tableT_ps[0:D, :],
                                              b2_sb[:, 0:1], None, ALU.add)
                taken.then_inc(bottom_ready, 1)

            def make_key(s):
                dve.wait_ge(digits_loaded[s % 2], fill(s // 2 + 1))
                bc = digit_bc[:, s % 2, :].rearrange("p (g b) -> p g b", g=DIGITS)
                dve.scalar_tensor_tensor(key[:, s % 2, :], bc[:, LO, :], partition_f[:, 0:1], bc[:, G1, :],
                                         ALU.is_equal, ALU.mult).then_inc(key_ready, 1)

            def make_onehot(j):
                s, g, i = place(j)
                if i == 0:
                    make_key(s)
                    dve.wait_ge(key_ready, s + 1)
                if j >= SLOTS:
                    dve.wait_ge(step_done, j - SLOTS + 1)
                dve.tensor_scalar(onehot[:, j % SLOTS, :], key[:, s % 2, :], float(g + 1), None, ALU.is_equal)\
                   .then_inc(onehot_ready, 1)

            def split(j):
                dve.wait_ge(high_ready, j + 1)
                dve.tensor_tensor(residual[:, j % SLOTS, :], projected_ps(j),
                                  parts[:, j % SLOTS, 0, :], ALU.subtract).then_inc(residual_ready, 1)
                dve.wait_ge(middle_ready, j + 1)
                dve.tensor_tensor(parts[:, j % SLOTS, 2, :], residual[:, j % SLOTS, :], parts[:, j % SLOTS, 1, :], ALU.subtract)\
                   .then_inc(parts_ready, 1)

            def pick(s):
                h = digit_bc[:, s % 2, HH * B:(HH + 1) * B]
                dve.wait_ge(step_done, (s + 1) * GROUPS)
                to = picked if s else picked_sum
                if s >= 2:
                    dve.wait_ge(picked_summed, s - 1)
                for q in range(BANKS):
                    cols = slice(q * BANK, (q + 1) * BANK)
                    dve.scalar_tensor_tensor(to[:, cols], h[:, cols], part_h_f[:, 0:1], looked_ps[q][:, :],
                                             ALU.is_equal, ALU.mult).then_inc(picked_ready, 1)
                if s:
                    dve.wait_ge(picked_ready, (s + 1) * BANKS)
                    dve.tensor_tensor(picked_sum[:, :], picked_sum[:, :], picked[:, :], ALU.add)\
                       .then_inc(picked_summed, 1)

            for j in range(LEAD):
                make_onehot(j)
                split(j)
            for j in range(STEPS):
                if j + LEAD < STEPS:
                    make_onehot(j + LEAD)
                    split(j + LEAD)
                if 1 <= j <= BANKS * BOTTOM_STAGES:
                    bottom_stage(j - 1)
                if (j + 1) % GROUPS == 0:
                    pick(j // GROUPS)

            dve.wait_ge(head_weights, fill(2))
            dve.wait_ge(hidden_ready, 1)
            link(dve.scalar_tensor_tensor(weighted[:, :, :],
                                          hidden_ps[:, 0:TILES * H_TOP].rearrange("p (t h) -> p t h", h=H_TOP),
                                          0.0, tw2_all[:, :, :], ALU.max, ALU.mult))
            dve.tensor_reduce(logits[:, :], weighted[:, :, :], AX.X, ALU.add).then_inc(logits_ready, 1)

        @block.tensor
        def _(pe):
            def hidden(tile):
                return hidden_ps[:, tile * H_TOP:(tile + 1) * H_TOP]

            pe.wait_ge(identity_ready, 1)
            pe.wait_ge(digits_ready, DIGITS)
            for q in range(BANKS):
                for k in range(PER_BANK):
                    last = pe.transpose(looked_ps[q][0:DIGITS * LOOKED_UP, k * P:(k + 1) * P],
                                        digit_f[:, q * PER_BANK + k, :, :].rearrange("p g s -> p (g s)"),
                                        identity[:, :])
                last.then_inc(digits_in_psum, 1)

            pe.wait_ge(ones_ready, 1)
            pe.wait_ge(top_weights, fill(6))
            pe.matmul(hidden_ps[:, 0:TILES * H_TOP], ones_row[:, :], tb1_row[:, :, :].rearrange("o t h -> o (t h)"),
                      start=True, stop=False)

            def bottom_stage(m):
                q, stage = divmod(m, BOTTOM_STAGES)
                if m == 0:
                    pe.wait_ge(dense_loaded, DMA)
                    pe.wait_ge(bottom_weights, fill(4))
                else:
                    pe.wait_ge(bottom_ready, m)
                if stage == 0:
                    for k in range(PER_BANK):
                        t = q * PER_BANK + k
                        last = pe.transpose(tableT_ps[0:DENSE, k * P:(k + 1) * P],
                                            dense_sb[:, t * DENSE:(t + 1) * DENSE], identity[:, :])
                elif stage == 1:
                    last = pe.matmul(tableT_ps[0:H_BOT, :], w1_sb[:, :], xT[:, :], start=True, stop=True)
                else:
                    last = pe.matmul(tableT_ps[0:D, :], w2_sb[:, :], bottomT[:, :], start=True, stop=True)
                last.then_inc(bottom_in_psum, 1)

            def add_dense():
                pe.wait_ge(bottom_ready, BANKS * BOTTOM_STAGES)
                for t in range(TILES):
                    pe.matmul(hidden(t), dense_outT[:, t * P:(t + 1) * P], tw1_dense[:, :], start=False, stop=False)

            def transpose_table(j):
                s, g, i = place(j)
                rows, blocks = extent(g)
                if i == 0:
                    pe.wait_ge(table_loaded[s % 2], fill(TABLE_LOADS * (s // 2 + 1)))
                if j:
                    pe.wait_ge(tableT_ready, j)
                if LEAD + 1 < j <= LEAD + 1 + BANKS * BOTTOM_STAGES:
                    pe.wait_ge(bottom_ready, j - LEAD - 1)
                for q in range(blocks):
                    for w in range(PAIRS):
                        k = q * PAIRS + w
                        last = pe.transpose(tableT_ps[:, k * P:k * P + rows],
                                            table[0:rows, s % 2, g * GROUP_BLOCKS + q, w * P:(w + 1) * P],
                                            identity[0:rows, 0:rows])
                last.then_inc(table_transposed, 1)

            def project(j):
                s, g, i = place(j)
                rows, blocks = extent(g)
                pe.wait_ge(tableT_ready, j + 1)
                if j >= 2:
                    pe.wait_ge(residual_ready, j - 1)
                for k in range(blocks * PAIRS):
                    last = pe.matmul(projected_ps(j)[0:rows, k * 2 * H_TOP:(k + 1) * 2 * H_TOP], tableT[:, k * P:k * P + rows],
                                     tw1_pair[:, s, :], start=True, stop=True)
                last.then_inc(projected, 1)

            def look_up(j, part):
                s, g, i = place(j)
                rows, blocks = extent(g)
                cols = blocks * RUN * H_TOP
                if part == 0:
                    pe.wait_ge(onehot_ready, j + 1)
                    pe.wait_ge(parts_ready, j + 1)
                for q in range(BANKS):
                    if part == 0 and i == 0 and s:
                        pe.wait_ge(picked_ready, (s - 1) * BANKS + q + 1)
                    last = pe.matmul(looked_ps[q][0:cols, :], parts[0:rows, j % SLOTS, part, 0:cols],
                                     onehot[0:rows, j % SLOTS, q * BANK:(q + 1) * BANK],
                                     start=i == 0 and part == 0, stop=i == GROUPS - 1 and part == SPLITS - 1)
                if part == SPLITS - 1:
                    last.then_inc(step_done, 1)

            def add_picked():
                pe.wait_ge(picked_summed, LOOKED_UP - 1)
                for t in range(TILES):
                    pe.matmul(hidden(t), picked_sum[:, t * P:(t + 1) * P], add_h[:, :], start=False, stop=False)

            def transpose_chunk(n):
                fields = len(chunk_fields(n % CHUNKS))
                pe.wait_ge(gathered[n % RING], fill(fields * (n // RING + 1)))
                if n >= 2:
                    pe.wait_ge(embT_ready, n - 1)
                pe.transpose(embT_ps(n)[0:fields * D, :], emb[:, n % RING, 0:fields * D], identity[:, :])\
                  .then_inc(emb_transposed, 1)

            def add_chunk(n):
                tile, c = divmod(n, CHUNKS)
                rows = len(chunk_fields(c)) * D
                pe.wait_ge(embT_ready, n + 1)
                last = pe.matmul(hidden(tile), embT[0:rows, n % 2, :], tw1_emb[0:rows, c, :], start=False,
                                 stop=n == ALL_CHUNKS - 1)
                if n == ALL_CHUNKS - 1:
                    last.then_inc(hidden_ready, 1)

            for j in range(LEAD):
                transpose_table(j)
                project(j)
            for j in range(STEPS):
                chunks = chunks_of_step[j]
                if j + LEAD < STEPS:
                    transpose_table(j + LEAD)
                for n in chunks[0:1]:
                    transpose_chunk(n)
                look_up(j, 0)
                if j + LEAD < STEPS:
                    project(j + LEAD)
                if 1 <= j <= BANKS * BOTTOM_STAGES:
                    bottom_stage(j - 1)
                if j == BANKS * BOTTOM_STAGES + 1:
                    add_dense()
                for n in chunks[0:1]:
                    add_chunk(n)
                for n in chunks[1:2]:
                    transpose_chunk(n)
                look_up(j, 1)
                for n in chunks[1:2]:
                    add_chunk(n)
                for n in chunks[2:]:
                    transpose_chunk(n)
                look_up(j, 2)
                for n in chunks[2:]:
                    add_chunk(n)
            for n in last_chunks:
                if n == ALL_CHUNKS - 1:
                    add_picked()
                transpose_chunk(n)
                add_chunk(n)


_INS = ["r_dense_x", "r_sparse_x"] + ["L0_rec_" + n for n in
        ("tables", "w1", "b1", "w2", "b2", "tw1", "tb1", "tw2", "tb2")]


def kernel(**inputs):
    import numpy as _np
    import concourse.bacc as _bacc
    from concourse import mybir as _mybir
    from concourse.bass_utils import run_bass_kernel_spmd as _run

    nc = _bacc.Bacc("TRN2", target_bir_lowering=False, num_devices=1)
    arrays, args = {}, []
    for name in _INS:
        a = _np.ascontiguousarray(inputs[name])
        arrays[f"in_{name}"] = a
        args.append(nc.dram_tensor(f"in_{name}", a.shape, _mybir.dt.from_np(a.dtype), kind="ExternalInput").ap())
    out_shape = (inputs["r_dense_x"].shape[0], inputs["L0_rec_tw2"].shape[1])
    out = nc.dram_tensor("out", out_shape, _mybir.dt.float32, kind="ExternalOutput").ap()
    embedding_mlp_kernel(nc, *args, out)
    r = _run(nc, [arrays], core_ids=[0])
    return r.results[0]["out"]
```

```python
import concourse.bass as bass
from concourse import mybir
from contextlib import ExitStack


def embedding_mlp_kernel(nc, dense_x, sparse_x, tables, w1, b1, w2, b2, tw1, tb1, tw2, tb2, out):
    f32, f32r, bf16, i32, u32 = mybir.dt.float32, mybir.dt.float32r, mybir.dt.bfloat16, mybir.dt.int32, mybir.dt.uint32
    ALU = mybir.AluOpType
    ACT = mybir.ActivationFunctionType
    AX = mybir.AxisListType

    P = 128
    B, DENSE = dense_x.shape
    F, CARD, D = tables.shape
    H_BOT, H_TOP = w1.shape[1], tw1.shape[1]
    TILES = B // P
    BANK = 512
    BANKS = B // BANK
    PER_BANK = BANK // P
    DMA = 16

    LOOKED_UP = 6
    GATHERED = F - LOOKED_UP
    PER_CHUNK = P // D
    CHUNKS = GATHERED // PER_CHUNK
    assert GATHERED % PER_CHUNK == 0
    RING = 2 * CHUNKS
    ALL_CHUNKS = TILES * CHUNKS

    RUN = 4
    BLOCK = RUN * P
    BLOCKS = CARD // BLOCK
    REST = (CARD - BLOCKS * BLOCK) // RUN
    H = P // H_TOP
    GROUP_BLOCKS = H // RUN
    GROUP_ROWS = GROUP_BLOCKS * BLOCK
    GROUPS = -(-CARD // GROUP_ROWS)
    PAIRS = RUN * D // P
    STEPS = LOOKED_UP * GROUPS
    SPLITS = 2
    LEAD = 2
    SLOTS = LEAD + 1
    DIGITS = 3
    LO, G1, HH = range(DIGITS)
    assert GROUP_ROWS == 1024 and BLOCK == 512 and REST * RUN + BLOCKS * BLOCK == CARD

    ARRIVE, AHEAD, MOST = 1.75, 10, 3
    chunks_of_step, taken = [], 0
    for j in range(STEPS):
        until = min(ALL_CHUNKS, taken + MOST, int(AHEAD + ARRIVE * j))
        chunks_of_step.append(list(range(taken, until)))
        taken = until
    last_chunks = range(taken, ALL_CHUNKS)
    LAST_TILE = TILES - 1
    assert taken < LAST_TILE * CHUNKS < ALL_CHUNKS

    def extent(g):
        blocks = min(GROUP_BLOCKS, BLOCKS + 1 - g * GROUP_BLOCKS)
        return (REST if g * GROUP_BLOCKS + blocks > BLOCKS else P), blocks

    sparse_v = sparse_x.rearrange("(p t) f -> p (t f)", t=TILES)
    dense_v = dense_x.rearrange("(p t) k -> p (t k)", t=TILES)
    rows_v = tables.rearrange("f c d -> (f c) d")
    out_v = out.rearrange("(p t) o -> p (t o)", t=TILES)
    digits_dram = nc.dram_tensor("digits_dram", [LOOKED_UP, DIGITS * B], bf16, kind="Internal").ap()

    ctx = ExitStack()
    with ctx:
        def sb(name, shape, dt=f32):
            return ctx.enter_context(nc.sbuf_tensor(name, shape, dt))

        def pb(name):
            return ctx.enter_context(nc.psum_tensor(name, [P, BANK], f32))

        def sem(name):
            return ctx.enter_context(nc.semaphore(name))

        sparse_sb = sb("sparse_sb", [P, TILES * F], i32)
        dense_sb = sb("dense_sb", [P, TILES * DENSE])
        w1_sb = sb("w1_sb", [DENSE, H_BOT])
        b1_sb = sb("b1_sb", [H_BOT, 1])
        w2_sb = sb("w2_sb", [H_BOT, D])
        b2_sb = sb("b2_sb", [D, 1])
        tw1_emb = sb("tw1_emb", [P, CHUNKS, H_TOP])
        tw1_dense = sb("tw1_dense", [D, H_TOP])
        tw1_pair = sb("tw1_pair", [P, LOOKED_UP, 2 * H_TOP])
        tb1_row = sb("tb1_row", [1, TILES, H_TOP])
        tw2_all = sb("tw2_all", [P, TILES, H_TOP])
        tb2_sb = sb("tb2_sb", [P, 1])
        identity = sb("identity", [P, P])
        ones_row = sb("ones_row", [1, P])
        warm_up = sb("warm_up", [1, P])
        field_base = sb("field_base", [P, TILES, F])
        partition = sb("partition", [P, 1], i32)
        partition_f = sb("partition_f", [P, 1])
        part_h = sb("part_h", [P, 1], i32)
        part_unit = sb("part_unit", [P, 1], i32)
        part_h_f = sb("part_h_f", [P, 1])
        part_unit_f = sb("part_unit_f", [P, 1])
        group_id = sb("group_id", [P, GROUPS])
        unit = sb("unit", [P, H_TOP])
        add_h = sb("add_h", [P, H_TOP])
        wrap = sb("wrap", [P, TILES * F])
        wrapped = sb("wrapped", [P, TILES * F])
        row_index = sb("row_index", [P, TILES * F], i32)
        local = sb("local", [P, TILES, LOOKED_UP], i32)
        digit_i = sb("digit_i", [P, 4, TILES, LOOKED_UP], i32)
        digit_f = sb("digit_f", [P, TILES, DIGITS, LOOKED_UP])
        digit_rows = sb("digit_rows", [DIGITS * LOOKED_UP, B], bf16)
        digit_bc = sb("digit_bc", [P, 2, DIGITS * B], bf16)
        xT = sb("xT", [DENSE, B])
        bottomT = sb("bottomT", [H_BOT, B])
        dense_outT = sb("dense_outT", [D, B])
        emb = sb("emb", [P, RING, P])
        embT = sb("embT", [P, MOST, P])
        table = sb("table", [P, 2, BLOCKS + 1, RUN * D])
        tableT = sb("tableT", [P, BANK])
        parts = sb("parts", [P, SLOTS, SPLITS, P], f32r)
        key = sb("key", [P, 2, B], bf16)
        onehot = sb("onehot", [P, SLOTS, B], f32r)
        picked = sb("picked", [P, B])
        picked_sum = sb("picked_sum", [P, B])
        weighted = sb("weighted", [P, TILES, H_TOP])
        logits = sb("logits", [P, TILES])
        result = sb("result", [P, TILES])

        hidden_ps = pb("hidden_ps")
        looked_ps = [pb(f"looked_ps{q}") for q in range(BANKS)]
        tableT_ps = pb("tableT_ps")
        shared_ps = pb("shared_ps")
        projected_ps = shared_ps[:, MOST * P:(MOST + 1) * P]
        group_id_ps = pb("group_id_ps")

        last_hidden_ps = looked_ps[0][:, 0:H_TOP]

        def last_bank(i):
            return (shared_ps, tableT_ps)[i % 2]

        sparse_loaded = sem("sparse_loaded")
        dense_loaded = sem("dense_loaded")
        bottom_weights = sem("bottom_weights")
        top_weights = sem("top_weights")
        head_weights = sem("head_weights")
        group_id_ready = sem("group_id_ready")
        pair_zeroed = sem("pair_zeroed")
        ones_ready = sem("ones_ready")
        base_ready = sem("base_ready")
        identity_zeroed = sem("identity_zeroed")
        identity_ready = sem("identity_ready")
        constants = sem("constants")
        dve_step = sem("dve_step")
        index_ready = sem("index_ready")
        digits_ready = sem("digits_ready")
        digits_in_psum = sem("digits_in_psum")
        digit_rows_ready = sem("digit_rows_ready")
        digits_stored = sem("digits_stored")
        digits_loaded = [sem(f"digits_loaded{k}") for k in range(2)]
        table_loaded = [sem(f"table_loaded{k}") for k in range(2)]
        early_loaded = sem("early_loaded")
        bottom_in_psum = sem("bottom_in_psum")
        bottom_ready = sem("bottom_ready")
        gathered = [sem(f"gathered{r}") for r in range(RING)]
        emb_transposed = sem("emb_transposed")
        embT_ready = sem("embT_ready")
        table_transposed = sem("table_transposed")
        tableT_ready = sem("tableT_ready")
        projected = sem("projected")
        high_ready = sem("high_ready")
        parts_ready = sem("parts_ready")
        key_ready = sem("key_ready")
        onehot_ready = sem("onehot_ready")
        step_done = sem("step_done")
        picked_ready = sem("picked_ready")
        picked_summed = sem("picked_summed")
        others_ready = sem("others_ready")
        last_ready = sem("last_ready")
        logits_ready = sem("logits_ready")
        result_ready = sem("result_ready")
        stored = sem("stored")

        TABLE_LOADS = 2
        EARLY = 4
        BOTTOM_STAGES = 3
        SUM_STEP = 3
        KEY_STEP = SUM_STEP + BANKS

        def fill(sem_value):
            return sem_value * DMA

        block = ctx.enter_context(nc.Block())

        @block.sync
        def _(sp):
            def load_blocks(s, first, last, loaded):
                rows = tables[GATHERED + s]
                sp.dma_start(table[:, s % 2, first:last, :],
                             rows[first * BLOCK:last * BLOCK, :].rearrange("(q p r) d -> p q (r d)", p=P, r=RUN))\
                  .then_inc(loaded, DMA)

            def load_table(s, first=0):
                rows = tables[GATHERED + s]
                load_blocks(s, first, BLOCKS, table_loaded[s % 2])
                sp.dma_start(table[0:REST, s % 2, BLOCKS, :],
                             rows[BLOCKS * BLOCK:CARD, :].rearrange("(p r) d -> p (r d)", r=RUN))\
                  .then_inc(table_loaded[s % 2], DMA)

            def load_digits(s):
                sp.dma_start(digit_bc[:, s % 2, :], digits_dram[s:s + 1, :].to_broadcast([P, DIGITS * B]))\
                  .then_inc(digits_loaded[s % 2], DMA)

            sp.dma_start(sparse_sb[:, :], sparse_v).then_inc(sparse_loaded, DMA)
            sp.dma_start(dense_sb[:, :], dense_v).then_inc(dense_loaded, DMA)
            sp.dma_start(w1_sb[:, :], w1).then_inc(bottom_weights, DMA)
            sp.dma_start(b1_sb[:, :], b1.rearrange("(h o) -> h o", o=1)).then_inc(bottom_weights, DMA)
            sp.dma_start(w2_sb[:, :], w2).then_inc(bottom_weights, DMA)
            sp.dma_start(b2_sb[:, :], b2.rearrange("(h o) -> h o", o=1)).then_inc(bottom_weights, DMA)
            load_blocks(0, 0, EARLY * GROUP_BLOCKS, early_loaded)
            sp.wait_ge(digit_rows_ready, BANKS)
            sp.dma_start(digits_dram.rearrange("s (g b) -> g s b", g=DIGITS), digit_rows[:, :])\
              .then_inc(digits_stored, DMA)
            sp.wait_ge(digits_stored, DMA)
            load_digits(0)
            load_table(0, EARLY * GROUP_BLOCKS)
            load_table(1)
            load_digits(1)
            for s in range(2, LOOKED_UP):
                sp.wait_ge(table_transposed, (s - 1) * GROUPS)
                load_table(s)
                sp.wait_ge(picked_ready, (s - 1) * BANKS)
                load_digits(s)
            sp.wait_ge(result_ready, 1)
            sp.dma_start(out_v, result[:, :]).then_inc(stored, DMA)
            sp.wait_ge(stored, DMA)

        @block.gpsimd
        def _(pool):
            pool.iota(field_base[:, :, :], [[0, TILES], [CARD, F]], base=0, channel_multiplier=0,
                      allow_small_or_imprecise_dtypes=True).then_inc(base_ready, 1)
            pool.memset(identity[:, :], 0.0).then_inc(identity_zeroed, 1)
            pool.wait_ge(identity_zeroed, 1)
            pool.affine_select(out=identity[:, :], in_=identity[:, :], compare_op=ALU.not_equal, fill=1.0,
                               base=0, pattern=[[-1, P]], channel_multiplier=1).then_inc(identity_ready, 1)
            pool.iota(partition[:, :], [[0, 1]], base=0, channel_multiplier=1).then_inc(constants, 1)
            pool.iota(group_id[:, :], [[1, GROUPS]], base=1, channel_multiplier=0,
                      allow_small_or_imprecise_dtypes=True).then_inc(constants, 1)
            pool.iota(unit[:, :], [[1, H_TOP]], base=0, channel_multiplier=0,
                      allow_small_or_imprecise_dtypes=True).then_inc(constants, 1)
            for n in range(ALL_CHUNKS):
                tile, c = divmod(n, CHUNKS)
                if n < 2 * CHUNKS and c == 0:
                    pool.wait_ge(index_ready, tile + 1)
                if n >= RING:
                    pool.wait_ge(emb_transposed, n - RING + 1)
                for e, f in enumerate(range(c * PER_CHUNK, (c + 1) * PER_CHUNK)):
                    pool.indirect_dma_start(
                        out=emb[:, n % RING, e * D:(e + 1) * D], out_offset=None, in_=rows_v,
                        in_offset=bass.IndirectOffsetOnAxis(
                            ap=row_index[:, tile * F + f:tile * F + f + 1].bitcast(u32), axis=0),
                    ).then_inc(gathered[n % RING], DMA)

        @block.scalar
        def _(act):
            act.dma_start(tb1_row[:, :, :], tb1.rearrange("(o t h) -> o t h", o=1, t=1)
                          .to_broadcast([1, TILES, H_TOP])).then_inc(top_weights, DMA)
            act.dma_start(tw1_emb[:, :, :], tw1[0:GATHERED * D, :].rearrange("(c p) h -> p c h", p=P))\
               .then_inc(top_weights, DMA)
            act.dma_start(tw1_dense[:, :], tw1[F * D:F * D + D, :]).then_inc(top_weights, DMA)
            act.wait_ge(pair_zeroed, 1)
            for e in range(2):
                act.dma_start(tw1_pair[e * D:(e + 1) * D, :, e * H_TOP:(e + 1) * H_TOP],
                              tw1[GATHERED * D:F * D, :].rearrange("(s d) h -> d s h", d=D))\
                   .then_inc(top_weights, DMA)
            act.dma_start(tw2_all[:, :, :], tw2.rearrange("(p t h) o -> p t (h o)", p=1, t=1)
                          .to_broadcast([P, TILES, H_TOP])).then_inc(head_weights, DMA)
            act.dma_start(tb2_sb[:, :], tb2.rearrange("(p o) -> p o", p=1).to_broadcast([P, 1]))\
               .then_inc(head_weights, DMA)

            act.wait_ge(ones_ready, 1)
            act.activation(warm_up[:, :], ones_row[:, :], ACT.Sigmoid)

            for q in range(BANKS):
                act.wait_ge(digits_in_psum, q + 1)
                act.activation(digit_rows[:, q * BANK:(q + 1) * BANK], looked_ps[q][0:DIGITS * LOOKED_UP, :],
                               ACT.Copy).then_inc(digit_rows_ready, 1)

            act.wait_ge(bottom_weights, fill(4))
            for stage in range(BOTTOM_STAGES):
                for q in range(BANKS):
                    cols = slice(q * BANK, (q + 1) * BANK)
                    act.wait_ge(bottom_in_psum, stage * BANKS + q + 1)
                    if stage == 0:
                        taken = act.activation(xT[:, cols], looked_ps[q][0:DENSE, :], ACT.Copy)
                    elif stage == 1:
                        taken = act.activation(bottomT[:, cols], looked_ps[q][0:H_BOT, :], ACT.Relu,
                                               bias=b1_sb[:, 0:1])
                    else:
                        taken = act.activation(dense_outT[:, cols], looked_ps[q][0:D, :], ACT.Identity,
                                               bias=b2_sb[:, 0:1])
                    taken.then_inc(bottom_ready, 1)

            def table_steps(j):
                act.wait_ge(table_transposed, j + 1)
                act.activation(tableT[:, :], tableT_ps[:, :], ACT.Copy).then_inc(tableT_ready, 1)

            def high(j):
                act.wait_ge(projected, j + 1)
                if j >= SLOTS:
                    act.wait_ge(step_done, j - SLOTS + 1)
                act.activation(parts[:, j % SLOTS, 0, :], projected_ps, ACT.Copy)\
                   .then_inc(high_ready, 1)

            def copy_chunks(some):
                act.wait_ge(emb_transposed, some[-1] + 1)
                act.activation(embT[:, 0:len(some), :],
                               shared_ps[:, 0:len(some) * P].rearrange("p (k n) -> p k n", n=P), ACT.Copy)\
                   .then_inc(embT_ready, len(some))

            for j in range(LEAD):
                table_steps(j)
                high(j)
            for j in range(STEPS):
                if j + LEAD < STEPS:
                    table_steps(j + LEAD)
                if chunks_of_step[j]:
                    copy_chunks(chunks_of_step[j])
                if j + LEAD < STEPS:
                    high(j + LEAD)
            for i, n in enumerate(last_chunks):
                act.wait_ge(emb_transposed, n + 1)
                act.activation(embT[:, i % 2, :], last_bank(i)[:, 0:P], ACT.Copy).then_inc(embT_ready, 1)
            act.wait_ge(head_weights, fill(2))
            act.wait_ge(logits_ready, 2)
            act.activation(result[:, :], logits[:, :], ACT.Sigmoid, bias=tb2_sb[:, 0:1]).then_inc(result_ready, 1)

        @block.vector
        def _(dve):
            done = [0]

            def link(instruction):
                done[0] += 1
                instruction.then_inc(dve_step, 1)
                dve.wait_ge(dve_step, done[0])

            dve.memset(tw1_pair[:, :, :], 0.0).then_inc(pair_zeroed, 1)
            dve.memset(ones_row[:, :], 1.0).then_inc(ones_ready, 1)
            dve.wait_ge(sparse_loaded, DMA)
            dve.wait_ge(base_ready, 1)
            base = field_base[:, :, :].rearrange("p t f -> p (t f)")
            for a, b in ((0, F), (F, TILES * F)):
                link(dve.tensor_scalar(wrap[:, a:b], sparse_sb[:, a:b], 0.0, float(CARD), ALU.is_lt, ALU.mult))
                link(dve.scalar_tensor_tensor(wrapped[:, a:b], sparse_sb[:, a:b], float(-CARD), wrap[:, a:b],
                                              ALU.max, ALU.add))
                dve.scalar_tensor_tensor(row_index[:, a:b], wrapped[:, a:b], float(CARD - 1), base[:, a:b],
                                         ALU.min, ALU.add).then_inc(index_ready, 1)

            link(dve.tensor_scalar(local[:, :, :],
                                   wrapped[:, :].rearrange("p (t f) -> p t f", f=F)[:, :, GATHERED:F],
                                   float(CARD - 1), None, ALU.min))
            g_i, lo_i, h1_i, h0_i = (digit_i[:, k, :, :] for k in range(4))
            link(dve.tensor_scalar(g_i, local[:, :, :], 10, None, ALU.logical_shift_right))
            link(dve.tensor_scalar(lo_i, local[:, :, :], 2, P - 1, ALU.logical_shift_right, ALU.bitwise_and))
            link(dve.tensor_scalar(h1_i, local[:, :, :], 7, RUN, ALU.logical_shift_right, ALU.bitwise_and))
            link(dve.tensor_scalar(h0_i, local[:, :, :], RUN - 1, None, ALU.bitwise_and))
            dve.tensor_scalar(digit_f[:, :, G1, :], g_i, 1.0, None, ALU.add).then_inc(digits_ready, 1)
            dve.tensor_copy(digit_f[:, :, LO, :], lo_i).then_inc(digits_ready, 1)
            dve.tensor_tensor(digit_f[:, :, HH, :], h1_i, h0_i, ALU.add).then_inc(digits_ready, 1)

            dve.wait_ge(constants, 3)
            dve.tensor_copy(group_id_ps[:, 0:GROUPS], group_id[:, :]).then_inc(group_id_ready, 1)
            link(dve.tensor_copy(partition_f[:, :], partition[:, :]))
            link(dve.tensor_scalar(part_h[:, :], partition[:, :], 4, None, ALU.logical_shift_right))
            link(dve.tensor_scalar(part_unit[:, :], partition[:, :], H_TOP - 1, None, ALU.bitwise_and))
            link(dve.tensor_copy(part_h_f[:, :], part_h[:, :]))
            link(dve.tensor_copy(part_unit_f[:, :], part_unit[:, :]))
            link(dve.tensor_scalar(add_h[:, :], unit[:, :], part_unit_f[:, 0:1], None, ALU.is_equal))

            def make_key(s, q):
                cols = slice(q * BANK, (q + 1) * BANK)
                dve.wait_ge(digits_loaded[s % 2], fill(s // 2 + 1))
                bc = digit_bc[:, s % 2, :].rearrange("p (g b) -> p g b", g=DIGITS)
                dve.scalar_tensor_tensor(key[:, s % 2, cols], bc[:, LO, cols], partition_f[:, 0:1],
                                         bc[:, G1, cols], ALU.is_equal, ALU.mult).then_inc(key_ready, 1)

            def make_onehot(j):
                s, g = divmod(j, GROUPS)
                if g == 0:
                    dve.wait_ge(key_ready, (s + 1) * BANKS)
                if j >= SLOTS:
                    dve.wait_ge(step_done, j - SLOTS + 1)
                if j == 0:
                    dve.wait_ge(group_id_ready, 1)
                dve.tensor_tensor(onehot[:, j % SLOTS, :], key[:, s % 2, :],
                                  group_id_ps[:, g:g + 1].to_broadcast([P, B]), ALU.is_equal)\
                   .then_inc(onehot_ready, 1)

            def low(j):
                dve.wait_ge(high_ready, j + 1)
                dve.tensor_tensor(parts[:, j % SLOTS, 1, :], projected_ps, parts[:, j % SLOTS, 0, :],
                                  ALU.subtract).then_inc(parts_ready, 1)

            def pick(s):
                h = digit_bc[:, s % 2, HH * B:(HH + 1) * B]
                dve.wait_ge(step_done, (s + 1) * GROUPS)
                to = picked if s else picked_sum
                if s >= 2:
                    dve.wait_ge(picked_summed, (s - 1) * BANKS)
                for q in range(BANKS):
                    cols = slice(q * BANK, (q + 1) * BANK)
                    dve.scalar_tensor_tensor(to[:, cols], h[:, cols], part_h_f[:, 0:1], looked_ps[q][:, :],
                                             ALU.is_equal, ALU.mult).then_inc(picked_ready, 1)

            def sum_picked(s, q):
                cols = slice(q * BANK, (q + 1) * BANK)
                dve.wait_ge(picked_ready, s * BANKS + q + 1)
                dve.tensor_tensor(picked_sum[:, cols], picked_sum[:, cols], picked[:, cols], ALU.add)\
                   .then_inc(picked_summed, 1)

            for q in range(BANKS):
                make_key(0, q)
            for j in range(LEAD):
                make_onehot(j)
                low(j)
            for j in range(STEPS):
                s, g = divmod(j, GROUPS)
                if g == 0 and s:
                    pick(s - 1)
                    low(j + LEAD)
                    make_onehot(j + LEAD)
                elif j + LEAD < STEPS:
                    make_onehot(j + LEAD)
                    low(j + LEAD)
                if s >= 2 and 0 <= g - SUM_STEP < BANKS:
                    sum_picked(s - 1, g - SUM_STEP)
                if s + 1 < LOOKED_UP and 0 <= g - KEY_STEP < BANKS:
                    make_key(s + 1, g - KEY_STEP)
            pick(LOOKED_UP - 1)
            for q in range(BANKS):
                sum_picked(LOOKED_UP - 1, q)

            def head(tiles, from_ps):
                link(dve.scalar_tensor_tensor(weighted[:, tiles, :], from_ps.rearrange("p (t h) -> p t h", h=H_TOP),
                                              0.0, tw2_all[:, tiles, :], ALU.max, ALU.mult))
                dve.tensor_reduce(logits[:, tiles], weighted[:, tiles, :], AX.X, ALU.add).then_inc(logits_ready, 1)

            dve.wait_ge(head_weights, fill(2))
            dve.wait_ge(others_ready, 1)
            head(slice(0, LAST_TILE), hidden_ps[:, 0:LAST_TILE * H_TOP])
            dve.wait_ge(last_ready, 1)
            head(slice(LAST_TILE, TILES), last_hidden_ps)

        @block.tensor
        def _(pe):
            def hidden(tile):
                return last_hidden_ps if tile == LAST_TILE else hidden_ps[:, tile * H_TOP:(tile + 1) * H_TOP]

            pe.wait_ge(identity_ready, 1)
            pe.wait_ge(digits_ready, DIGITS)
            for q in range(BANKS):
                for k in range(PER_BANK):
                    last = pe.transpose(looked_ps[q][0:DIGITS * LOOKED_UP, k * P:(k + 1) * P],
                                        digit_f[:, q * PER_BANK + k, :, :].rearrange("p g s -> p (g s)"),
                                        identity[:, :])
                last.then_inc(digits_in_psum, 1)

            pe.wait_ge(ones_ready, 1)
            pe.wait_ge(top_weights, fill(5))
            pe.matmul(hidden_ps[:, 0:LAST_TILE * H_TOP], ones_row[:, :],
                      tb1_row[:, 0:LAST_TILE, :].rearrange("o t h -> o (t h)"), start=True, stop=False)

            pe.wait_ge(dense_loaded, DMA)
            pe.wait_ge(bottom_weights, fill(4))
            for stage in range(BOTTOM_STAGES):
                for q in range(BANKS):
                    cols = slice(q * BANK, (q + 1) * BANK)
                    if stage == 0:
                        pe.wait_ge(digit_rows_ready, q + 1)
                        for k in range(PER_BANK):
                            t = q * PER_BANK + k
                            last = pe.transpose(looked_ps[q][0:DENSE, k * P:(k + 1) * P],
                                                dense_sb[:, t * DENSE:(t + 1) * DENSE], identity[:, :])
                    else:
                        pe.wait_ge(bottom_ready, (stage - 1) * BANKS + q + 1)
                        if stage == 1:
                            last = pe.matmul(looked_ps[q][0:H_BOT, :], w1_sb[:, :], xT[:, cols],
                                             start=True, stop=True)
                        else:
                            last = pe.matmul(looked_ps[q][0:D, :], w2_sb[:, :], bottomT[:, cols],
                                             start=True, stop=True)
                    last.then_inc(bottom_in_psum, 1)

            def add_dense(t):
                if t % PER_BANK == 0:
                    pe.wait_ge(bottom_ready, (BOTTOM_STAGES - 1) * BANKS + t // PER_BANK + 1)
                pe.matmul(hidden(t), dense_outT[:, t * P:(t + 1) * P], tw1_dense[:, :], start=False, stop=False)

            def transpose_table(j):
                s, g = divmod(j, GROUPS)
                rows, blocks = extent(g)
                if s == 0 and g == 0:
                    pe.wait_ge(early_loaded, DMA)
                elif g == 0 or (s == 0 and g == EARLY):
                    pe.wait_ge(table_loaded[s % 2], fill(TABLE_LOADS * (s // 2 + 1)))
                if j:
                    pe.wait_ge(tableT_ready, j)
                for q in range(blocks):
                    for w in range(PAIRS):
                        k = q * PAIRS + w
                        last = pe.transpose(tableT_ps[:, k * P:k * P + rows],
                                            table[0:rows, s % 2, g * GROUP_BLOCKS + q, w * P:(w + 1) * P],
                                            identity[0:rows, 0:rows])
                last.then_inc(table_transposed, 1)

            def project(j, chunks):
                s, g = divmod(j, GROUPS)
                rows, blocks = extent(g)
                pe.wait_ge(tableT_ready, j + 1)
                if chunks:
                    pe.wait_ge(embT_ready, chunks)
                if j:
                    pe.wait_ge(parts_ready, j)
                for k in range(blocks * PAIRS):
                    last = pe.matmul(projected_ps[0:rows, k * 2 * H_TOP:(k + 1) * 2 * H_TOP],
                                     tableT[:, k * P:k * P + rows], tw1_pair[:, s, :], start=True, stop=True)
                last.then_inc(projected, 1)

            def look_up(j, part):
                s, g = divmod(j, GROUPS)
                rows, blocks = extent(g)
                if part == 0:
                    pe.wait_ge(onehot_ready, j + 1)
                    pe.wait_ge(parts_ready, j + 1)
                for q in range(BANKS):
                    if part == 0 and j == 0:
                        pe.wait_ge(bottom_ready, (BOTTOM_STAGES - 1) * BANKS + q + 1)
                    if part == 0 and g == 0 and s:
                        pe.wait_ge(picked_ready, (s - 1) * BANKS + q + 1)
                    last = pe.matmul(looked_ps[q][:, :], parts[0:rows, j % SLOTS, part, :],
                                     onehot[0:rows, j % SLOTS, q * BANK:(q + 1) * BANK],
                                     start=g == 0 and part == 0, stop=g == GROUPS - 1 and part == SPLITS - 1)
                if part == SPLITS - 1:
                    last.then_inc(step_done, 1)

            def add_picked():
                pe.wait_ge(picked_summed, (LOOKED_UP - 1) * BANKS)
                for t in range(LAST_TILE):
                    last = pe.matmul(hidden(t), picked_sum[:, t * P:(t + 1) * P], add_h[:, :],
                                     start=False, stop=t == LAST_TILE - 1)
                last.then_inc(others_ready, 1)

            def open_last_tile():
                t = LAST_TILE
                pe.matmul(hidden(t), ones_row[:, :], tb1_row[:, 0, :], start=True, stop=False)
                add_dense(t)
                pe.matmul(hidden(t), picked_sum[:, t * P:(t + 1) * P], add_h[:, :], start=False, stop=False)

            def transpose_chunks(some, groups):
                for k, n in enumerate(some):
                    pe.wait_ge(gathered[n % RING], fill(PER_CHUNK * (n // RING + 1)))
                    if k == 0:
                        pe.wait_ge(parts_ready, groups)
                        if n:
                            pe.wait_ge(embT_ready, n)
                    pe.transpose(shared_ps[:, k * P:(k + 1) * P], emb[:, n % RING, :], identity[:, :])\
                      .then_inc(emb_transposed, 1)

            def add_chunks(some):
                for k, n in enumerate(some):
                    tile, c = divmod(n, CHUNKS)
                    if k == 0:
                        pe.wait_ge(embT_ready, some[-1] + 1)
                    pe.matmul(hidden(tile), embT[:, k, :], tw1_emb[:, c, :], start=False, stop=False)

            def add_last(i):
                n = last_chunks[i]
                tile, c = divmod(n, CHUNKS)
                if n == LAST_TILE * CHUNKS:
                    add_picked()
                    open_last_tile()
                pe.wait_ge(embT_ready, n + 1)
                last = pe.matmul(hidden(tile), embT[:, i % 2, :], tw1_emb[:, c, :], start=False,
                                 stop=n == ALL_CHUNKS - 1)
                if n == ALL_CHUNKS - 1:
                    last.then_inc(last_ready, 1)

            for j in range(LEAD):
                transpose_table(j)
                project(j, 0)
            waiting, taken = [], 0
            for j in range(STEPS):
                if j + LEAD < STEPS:
                    transpose_table(j + LEAD)
                add_chunks(waiting)
                if 1 <= j <= LAST_TILE:
                    add_dense(j - 1)
                waiting = chunks_of_step[j]
                taken += len(waiting)
                transpose_chunks(waiting, min(j + LEAD, STEPS))
                boundary = j > 0 and j % GROUPS == 0
                if not boundary:
                    look_up(j, 0)
                if j + LEAD < STEPS:
                    project(j + LEAD, taken)
                if boundary:
                    look_up(j, 0)
                look_up(j, 1)
            add_chunks(waiting)
            for i, n in enumerate(last_chunks):
                pe.wait_ge(gathered[n % RING], fill(PER_CHUNK * (n // RING + 1)))
                if i == 0:
                    pe.wait_ge(parts_ready, STEPS)
                    pe.wait_ge(embT_ready, n)
                elif i >= 2:
                    pe.wait_ge(embT_ready, n - 1)
                pe.transpose(last_bank(i)[:, 0:P], emb[:, n % RING, :], identity[:, :])\
                  .then_inc(emb_transposed, 1)
                if i:
                    add_last(i - 1)
            add_last(len(last_chunks) - 1)


_INS = ["r_dense_x", "r_sparse_x"] + ["L0_rec_" + n for n in
        ("tables", "w1", "b1", "w2", "b2", "tw1", "tb1", "tw2", "tb2")]


def kernel(**inputs):
    import numpy as _np
    import concourse.bacc as _bacc
    from concourse import mybir as _mybir
    from concourse.bass_utils import run_bass_kernel_spmd as _run

    nc = _bacc.Bacc("TRN2", target_bir_lowering=False, num_devices=1)
    arrays, args = {}, []
    for name in _INS:
        a = _np.ascontiguousarray(inputs[name])
        arrays[f"in_{name}"] = a
        args.append(nc.dram_tensor(f"in_{name}", a.shape, _mybir.dt.from_np(a.dtype), kind="ExternalInput").ap())
    out_shape = (inputs["r_dense_x"].shape[0], inputs["L0_rec_tw2"].shape[1])
    out = nc.dram_tensor("out", out_shape, _mybir.dt.float32, kind="ExternalOutput").ap()
    embedding_mlp_kernel(nc, *args, out)
    r = _run(nc, [arrays], core_ids=[0])
    return r.results[0]["out"]
```
